# Optimizing a Trainium2 kernel written in Bass

```python
import numpy as np
import jax
import jax.numpy as jnp

def _softmax(x, axis=-1):
    return jax.nn.softmax(x, axis=axis)

def _gelu(x):
    return jax.nn.gelu(x, approximate=True)

def _silu(x):
    return jax.nn.silu(x)

def _sigmoid(x):
    return jax.nn.sigmoid(x)

def _layernorm(x, axis=-1, eps=1e-05):
    m = jnp.mean(x, axis=axis, keepdims=True)
    v = jnp.var(x, axis=axis, keepdims=True)
    return (x - m) / jnp.sqrt(v + eps)

def _scatter_add(tgt, idx, src, axis=0):
    return tgt.at[idx].add(src)

def _segment_sum(src, seg, n):
    return jax.ops.segment_sum(src, seg, n)
kernel_name = 'mk_macaron_d1_jaxref_r8_eea6a8'

def setup_inputs(seed: int=0):
    np.random.seed(seed)
    _w = jnp.asarray

    def _L0_attn_setup():
        import jax, jax.numpy as jnp
        import numpy as np
        DIM = 128
        HEADS = 16
        EPS = 1e-12
        key = jax.random.key(seed)
        ks = jax.random.split(key, 6)
        b, n, dim, h = (2, 256, DIM, HEADS)
        x = jax.random.normal(ks[0], (b, n, dim), dtype=jnp.float32)
        w_qkv = jax.random.normal(ks[1], (3 * dim, dim), dtype=jnp.float32) / np.sqrt(dim)
        w_out = jax.random.normal(ks[2], (dim, dim), dtype=jnp.float32) / np.sqrt(dim)
        b_out = jax.random.normal(ks[3], (dim,), dtype=jnp.float32) * 0.02
        norm_g = jnp.ones((1, h, 1, 1), dtype=jnp.float32)
        norm_b = jnp.zeros((1, h, 1, 1), dtype=jnp.float32)
        return {'x': x, 'w_qkv': w_qkv, 'w_out': w_out, 'b_out': b_out, 'norm_g': norm_g, 'norm_b': norm_b}
    _L0_attn_in = _L0_attn_setup()

    def _L0_ffn_setup():
        import jax, jax.numpy as jnp
        import numpy as np
        from jax import lax
        D_MODEL = 128
        INTER = 128
        N_EXPERTS = 8
        TOP_K = 2
        ROUTE_SCALE = 1.0
        B, S = (2, 512)
        key = jax.random.key(seed)
        ks = jax.random.split(key, 16)
        sc_d = 1.0 / np.sqrt(D_MODEL)
        sc_f = 1.0 / np.sqrt(INTER)
        inp = {'x': jax.random.normal(ks[0], (B, S, D_MODEL), dtype=jnp.float32), 'gate_w': jax.random.normal(ks[1], (N_EXPERTS, D_MODEL), dtype=jnp.float32) * sc_d, 'w1': jax.random.normal(ks[2], (N_EXPERTS, D_MODEL, INTER), dtype=jnp.float32) * sc_d, 'b1': jnp.zeros((N_EXPERTS, INTER), dtype=jnp.float32), 'w2': jax.random.normal(ks[3], (N_EXPERTS, INTER, D_MODEL), dtype=jnp.float32) * sc_f, 'b2': jnp.zeros((N_EXPERTS, D_MODEL), dtype=jnp.float32), 'w3': jax.random.normal(ks[4], (N_EXPERTS, D_MODEL, INTER), dtype=jnp.float32) * sc_d, 'b3': jnp.zeros((N_EXPERTS, INTER), dtype=jnp.float32), 'sw1': jax.random.normal(ks[5], (D_MODEL, INTER), dtype=jnp.float32) * sc_d, 'sb1': jnp.zeros((INTER,), dtype=jnp.float32), 'sw2': jax.random.normal(ks[6], (INTER, D_MODEL), dtype=jnp.float32) * sc_f, 'sb2': jnp.zeros((D_MODEL,), dtype=jnp.float32), 'sw3': jax.random.normal(ks[7], (D_MODEL, INTER), dtype=jnp.float32) * sc_d, 'sb3': jnp.zeros((INTER,), dtype=jnp.float32)}
        return inp
    _L0_ffn_in = _L0_ffn_setup()
    _d = {'L0_attn_x': _L0_attn_in['x'], 'L0_attn_w_qkv': _L0_attn_in['w_qkv'], 'L0_attn_w_out': _L0_attn_in['w_out'], 'L0_attn_b_out': _L0_attn_in['b_out'], 'L0_attn_norm_g': _L0_attn_in['norm_g'], 'L0_attn_norm_b': _L0_attn_in['norm_b'], 'L0_ffn_gate_w': _L0_ffn_in['gate_w'], 'L0_ffn_w1': _L0_ffn_in['w1'], 'L0_ffn_b1': _L0_ffn_in['b1'], 'L0_ffn_w2': _L0_ffn_in['w2'], 'L0_ffn_b2': _L0_ffn_in['b2'], 'L0_ffn_w3': _L0_ffn_in['w3'], 'L0_ffn_b3': _L0_ffn_in['b3'], 'L0_ffn_sw1': _L0_ffn_in['sw1'], 'L0_ffn_sb1': _L0_ffn_in['sb1'], 'L0_ffn_sw2': _L0_ffn_in['sw2'], 'L0_ffn_sb2': _L0_ffn_in['sb2'], 'L0_ffn_sw3': _L0_ffn_in['sw3'], 'L0_ffn_sb3': _L0_ffn_in['sb3']}
    _x0 = _d['L0_attn_x']
    _d['L0_attn_x'] = jax.random.normal(jax.random.fold_in(jax.random.key(seed), 1), (4, 512, 128), dtype=_x0.dtype)
    del _x0
    return _d

def reference(L0_attn_x, L0_attn_w_qkv, L0_attn_w_out, L0_attn_b_out, L0_attn_norm_g, L0_attn_norm_b, L0_ffn_gate_w, L0_ffn_w1, L0_ffn_b1, L0_ffn_w2, L0_ffn_b2, L0_ffn_w3, L0_ffn_b3, L0_ffn_sw1, L0_ffn_sb1, L0_ffn_sw2, L0_ffn_sb2, L0_ffn_sw3, L0_ffn_sb3):

    def _L0_attn_ref(x, w_qkv, w_out, b_out, norm_g, norm_b):
        import jax, jax.numpy as jnp
        import numpy as np
        DIM = 128
        HEADS = 16
        EPS = 1e-12
        b, n, dim = x.shape
        h = HEADS
        d = dim // h
        qkv = jnp.einsum('bnm,om->bno', x, w_qkv)
        qkv = qkv.reshape(b, n, 3, h, d)
        q, k, v = [jnp.transpose(qkv[:, :, i], (0, 2, 1, 3)) for i in range(3)]
        dots = jnp.einsum('bhid,bhjd->bhij', q, k)
        norm = jnp.sqrt(jnp.sum(dots * dots, axis=-1, keepdims=True))
        attn = dots / jnp.maximum(norm, EPS) * norm_g + norm_b
        out = jnp.einsum('bhij,bhjd->bhid', attn, v)
        out = jnp.transpose(out, (0, 2, 1, 3)).reshape(b, n, dim)
        return jnp.einsum('bnm,om->bno', out, w_out) + b_out

    def _L0_ffn_ref(x, gate_w, w1, b1, w2, b2, w3, b3, sw1, sb1, sw2, sb2, sw3, sb3):
        import jax, jax.numpy as jnp
        import numpy as np
        from jax import lax
        D_MODEL = 128
        INTER = 128
        N_EXPERTS = 8
        TOP_K = 2
        ROUTE_SCALE = 1.0
        B, S = (2, 512)
        Bx, Sx, D = x.shape
        xt = x.reshape(-1, D)
        scores = jax.nn.softmax((xt @ gate_w.T).astype(jnp.float32), axis=-1)
        top_vals, top_idx = lax.top_k(scores, TOP_K)
        weights = (top_vals * ROUTE_SCALE).astype(x.dtype)
        combine = jnp.sum(jax.nn.one_hot(top_idx, N_EXPERTS, dtype=x.dtype) * weights[..., None], axis=1)

        def body(acc, p):
            W1, B1, W2, B2, W3, B3, c = p
            h = jax.nn.silu(xt @ W1 + B1) * (xt @ W3 + B3)
            return (acc + c[:, None] * (h @ W2 + B2), None)
        y, _ = lax.scan(body, jnp.zeros_like(xt), (w1, b1, w2, b2, w3, b3, combine.T))
        z = jax.nn.silu(xt @ sw1 + sb1) * (xt @ sw3 + sb3) @ sw2 + sb2
        return (y + z).reshape(Bx, Sx, D)
    x = L0_attn_x
    x = x + 0.5 * _L0_ffn_ref(_layernorm(x, axis=-1), L0_ffn_gate_w, L0_ffn_w1, L0_ffn_b1, L0_ffn_w2, L0_ffn_b2, L0_ffn_w3, L0_ffn_b3, L0_ffn_sw1, L0_ffn_sb1, L0_ffn_sw2, L0_ffn_sb2, L0_ffn_sw3, L0_ffn_sb3)
    x = x + _L0_attn_ref(_layernorm(x, axis=-1), L0_attn_w_qkv, L0_attn_w_out, L0_attn_b_out, L0_attn_norm_g, L0_attn_norm_b)
    x = x + 0.5 * _L0_ffn_ref(_layernorm(x, axis=-1), L0_ffn_gate_w, L0_ffn_w1, L0_ffn_b1, L0_ffn_w2, L0_ffn_b2, L0_ffn_w3, L0_ffn_b3, L0_ffn_sw1, L0_ffn_sb1, L0_ffn_sw2, L0_ffn_sb2, L0_ffn_sw3, L0_ffn_sb3)
    return x

_drawn_inputs = setup_inputs


def setup_inputs(seed=0):
    import zlib

    import numpy as np

    out = dict(_drawn_inputs(seed))
    spreads = {'L0_attn_norm_g': (1.0, 0.2),
     'L0_attn_norm_b': (0.0, 0.1),
     'L0_ffn_b1': (0.0, 0.469),
     'L0_ffn_b2': (0.0, 0.1),
     'L0_ffn_b3': (0.0, 0.3),
     'L0_ffn_sb1': (0.0, 0.1),
     'L0_ffn_sb2': (0.0, 0.1),
     'L0_ffn_sb3': (0.0, 0.1)}
    factors = {'L0_attn_b_out': 8.0}
    for name, (base, spread) in spreads.items():
        noise = np.random.default_rng([zlib.crc32(name.encode()), seed]).standard_normal(out[name].shape)
        drawn = base * np.exp(spread * noise) if base else spread * noise
        out[name] = jnp.asarray(drawn.astype(out[name].dtype))
    for name, factor in factors.items():
        out[name] = (out[name] * factor).astype(out[name].dtype)
    return out
```

```python
from contextlib import ExitStack

import concourse.bass as bass
from concourse import mybir

F32 = mybir.dt.float32
F32R = mybir.dt.float32r
BF16 = mybir.dt.bfloat16
ALU = mybir.AluOpType
ACT = mybir.ActivationFunctionType
AX_X = mybir.AxisListType.X

P = 128
LN_EPS = 1e-5
NORM_EPS = 1e-12


def macaron_kernel(
    nc: bass.Bass,
    x_in: bass.AP,
    wqkv_t: bass.AP,
    wout_t: bass.AP,
    b_out: bass.AP,
    norm_g: bass.AP,
    norm_b: bass.AP,
    gate_t: bass.AP,
    w1: bass.AP,
    bias_t: bass.AP,
    w2: bass.AP,
    b2: bass.AP,
    w3: bass.AP,
    sw1: bass.AP,
    sw2: bass.AP,
    sb2: bass.AP,
    sw3: bass.AP,
    out: bass.AP,
    heads: int,
):
    NB, SEQ, D = x_in.shape
    NE = w1.shape[0]
    HEADS = heads
    HD = D // HEADS
    TOK = NB * SEQ
    TB = SEQ // P
    NT = NB * TB
    SETS = NE + 1
    assert D == P and w1.shape[2] == P and NB == 4 and SEQ == 512 and NE % 2 == 0 and NT * NE == P

    c_dram = [nc.dram_tensor(f"combine_{f}", (NE, TOK), F32, kind="Internal").ap() for f in range(2)]

    with ExitStack() as ctx:
        def sb(name, shape, dt=F32):
            return ctx.enter_context(nc.sbuf_tensor(name, shape, dt))

        def psum(name, shape):
            return ctx.enter_context(nc.psum_tensor(name, shape, F32))

        def sem(name):
            return ctx.enter_context(nc.semaphore(name))

        x = sb("x", [P, NT, D])
        xh = sb("xh", [P, TOK], F32R)
        xl = sb("xl", [P, TOK], F32R)
        w13_raw = sb("w13_raw", [P, SETS + 1, 2, P])
        w2_raw = sb("w2_raw", [P, SETS + 1, P])
        w13h = [sb(f"w13h{p}", [P, 2, P], F32R) for p in range(2)]
        w13l = [sb(f"w13l{p}", [P, 2, P], F32R) for p in range(2)]
        w2h = [sb(f"w2h{p}", [P, P], F32R) for p in range(2)]
        w2l = [sb(f"w2l{p}", [P, P], F32R) for p in range(2)]
        bias_raw = sb("bias_raw", [P, SETS + 1, 2])
        bias13 = [sb(f"bias13{p}", [P, 2]) for p in range(2)]
        b2s = sb("b2s", [NE, P])
        sb2s = sb("sb2s", [P, 1])
        gate_raw = sb("gate_raw", [P, NE])
        gate_h = sb("gate_h", [P, NE], F32R)
        gate_l = sb("gate_l", [P, NE], F32R)
        wqkv = sb("wqkv", [P, 3 * D])
        wout = sb("wout", [P, D])
        bout_rows = sb("bout_rows", [P, D])
        ng = sb("ng", [P, 1])
        nb = sb("nb", [P, 1])
        ident = sb("ident", [P, P])
        head_mask = sb("head_mask", [P, HEADS, HD])
        tie_order = sb("tie_order", [P, NT, NE])
        zeros = sb("zeros", [P, 512], BF16)
        minus_half = sb("minus_half", [P, TB])
        stats = sb("stats", [P, 2, TB, 6])
        moments = sb("moments", [P, 2, TB, 2])
        var_eps = sb("var_eps", [P, 2, TB])
        rstd = sb("rstd", [P, 2, TB])
        wait_carrier = sb("wait_carrier", [P, 1])
        xn = [sb(f"xn{p}", [P, TB, D + 2]) for p in range(2)]
        small = [sb(f"small{k}", [P, NT]) for k in range(6)]
        g_d = sb("g_d", [P, NT, NE])
        g_e = sb("g_e", [P, NT, NE])
        g_p = sb("g_p", [P, NT, NE])
        g_w = sb("g_w", [P, NT, NE])
        g_v = sb("g_v", [P, NT, NE])
        g_s1 = sb("g_s1", [P, NT, NE])
        g_p2 = sb("g_p2", [P, NT, NE])
        g_s2 = sb("g_s2", [P, NT, NE])
        g_sel = sb("g_sel", [P, NT, NE])
        g_c = sb("g_c", [P, NE, NT])
        c_rows = sb("c_rows", [P, P])
        cT = sb("cT", [NE, TOK])
        cb = [sb(f"cb{p}", [P, TOK]) for p in range(2)]
        s_t = [sb(f"s_t{k}", [P, SEQ]) for k in range(2)]
        u_t = [sb(f"u_t{k}", [P, SEQ]) for k in range(2)]
        hh = [sb(f"hh{k}", [P, SEQ], F32R) for k in range(NB)]
        hl = [sb(f"hl{k}", [P, SEQ], F32R) for k in range(NB)]
        yT = [sb(f"yT{k}", [P, SEQ]) for k in range(NB)]
        a_xT = [sb(f"a_xT{p}", [P, SEQ]) for p in range(2)]
        a_S = [sb(f"a_S{p}", [P, D + 2]) for p in range(2)]
        a_T = [sb(f"a_T{p}", [P, 2 * D]) for p in range(2)]
        a_bv = [sb(f"a_bv{p}", [P, 1]) for p in range(2)]
        a_G = [sb(f"a_G{p}", [P, D]) for p in range(2)]
        a_N = [sb(f"a_N{p}", [P, D]) for p in range(2)]
        a_Q = [sb(f"a_Q{p}", [P, SEQ]) for p in range(2)]
        a_P = [sb(f"a_P{p}", [P, SEQ]) for p in range(2)]
        a_n2 = [sb(f"a_n2{p}", [P, TB, HEADS]) for p in range(2)]
        a_nr = [sb(f"a_nr{p}", [P, TB, HEADS]) for p in range(2)]
        a_inv = [sb(f"a_inv{p}", [P, TB, HEADS]) for p in range(2)]
        a_A = [sb(f"a_A{p}", [P, TB, D]) for p in range(2)]
        a_aT = [sb(f"a_aT{p}", [P, SEQ]) for p in range(2)]

        work = [psum(f"work{k}", [P, 512]) for k in range(4)]
        yps = [psum(f"yps{k}", [P, 512]) for k in range(4)]
        bank = [[work[2 * p], work[2 * p + 1], yps[2 * p], yps[2 * p + 1]] for p in range(2)]
        logits = yps[3][:, 0:P]
        c_tr = yps[3][:, P:2 * P]

        x_in_sem = [sem(f"x_landed{b}") for b in range(NB)]
        w_landed = [sem(f"w_landed{k}") for k in range(3)]
        small_landed = sem("small_landed")
        attn_landed = sem("attn_landed")
        const_step = sem("const_step")
        consts = sem("consts")
        stats_done = sem("stats_done")
        moments_done = sem("moments_done")
        var_done = sem("var_done")
        rstd_done = sem("rstd_done")
        xn_done = sem("xn_done")
        xT_done = sem("xT_done")
        xh_done = sem("xh_done")
        xl_done = sem("xl_done")
        gate_w_done = sem("gate_w_done")
        logits_done = sem("logits_done")
        gate_step = sem("gate_step")
        gate_centred = sem("gate_centred")
        gate_exp = sem("gate_exp")
        combine_done = sem("combine_done")
        c_tr_done = sem("c_tr_done")
        c_rows_done = sem("c_rows_done")
        c_stored = sem("c_stored")
        cT_landed = sem("cT_landed")
        cb_landed = [[sem(f"cb_landed{p}{b}") for b in range(NB)] for p in range(2)]
        w13h_done = sem("w13h_done")
        w13l_done = sem("w13l_done")
        w2h_done = sem("w2h_done")
        w2l_done = sem("w2l_done")
        gate_half = sem("gate_half")
        lin_half = sem("lin_half")
        silu_done = sem("silu_done")
        weighted = sem("weighted")
        u_done = sem("u_done")
        hh_done = sem("hh_done")
        hl_even = sem("hl_even")
        hl_odd = sem("hl_odd")
        down_done = sem("down_done")
        y_done = sem("y_done")
        yT_done = sem("yT_done")
        y_back = sem("y_back")
        resid = sem("resid")
        bout_added = sem("bout_added")
        a_xT_ps = sem("a_xT_ps")
        a_S_ps = sem("a_S_ps")
        a_xT_sb = sem("a_xT_sb")
        a_S_sb = sem("a_S_sb")
        a_T_ps = sem("a_T_ps")
        a_Q_ps = sem("a_Q_ps")
        a_T_sb = sem("a_T_sb")
        a_Q_sb = sem("a_Q_sb")
        a_GN_ps = sem("a_GN_ps")
        a_GN_sb = sem("a_GN_sb")
        a_U_ps = sem("a_U_ps")
        a_R_ps = sem("a_R_ps")
        a_P_sb = sem("a_P_sb")
        a_n_ps = sem("a_n_ps")
        a_n2_sb = sem("a_n2_sb")
        a_root = sem("a_root")
        a_inv_sb = sem("a_inv_sb")
        a_A_sb = sem("a_A_sb")
        a_At_ps = sem("a_At_ps")
        a_aT_sb = sem("a_aT_sb")
        a_O_ps = sem("a_O_ps")
        stored = sem("stored")

        UF = NB * SETS
        RF = NB * NE

        x_tok = x_in.rearrange("b s d -> (b s) d").rearrange("(t p) d -> p t d", p=P)
        out_tok = out.rearrange("b s d -> (b s) d").rearrange("(t p) d -> p t d", p=P)

        block = ctx.enter_context(nc.Block())

        @block.sync
        def _(sp):
            for b in range(NB):
                sp.dma_start(x[:, TB * b:TB * b + TB, :], x_tok[:, TB * b:TB * b + TB, :]).then_inc(x_in_sem[b], 16)
                if b == 0:
                    sp.dma_start(gate_raw[:], gate_t).then_inc(small_landed, 16)
                    sp.dma_start(bias_raw[:], bias_t).then_inc(small_landed, 16)
                    sp.dma_start(b2s[:], b2).then_inc(small_landed, 16)
                    sp.dma_start(sb2s[:], sb2).then_inc(small_landed, 16)
                    sp.dma_start(w13_raw[:, 0, 0, :], sw1).then_inc(w_landed[0], 16)
                    sp.dma_start(w13_raw[:, 0, 1, :], sw3).then_inc(w_landed[0], 16)
                    sp.dma_start(w2_raw[:, 0, :], sw2).then_inc(w_landed[0], 16)
            for k, (e0, e1) in enumerate([(0, 2), (2, NE)]):
                for w, dst in ((w1, w13_raw[:, 1 + e0:1 + e1, 0, :]), (w3, w13_raw[:, 1 + e0:1 + e1, 1, :]),
                               (w2, w2_raw[:, 1 + e0:1 + e1, :])):
                    sp.dma_start(dst, w[e0:e1].rearrange("e i o -> i e o")).then_inc(w_landed[1 + k], 16)
            sp.dma_start(w13_raw[:, SETS, 0, :], sw1).then_inc(w_landed[2], 16)
            sp.dma_start(w13_raw[:, SETS, 1, :], sw3).then_inc(w_landed[2], 16)
            sp.dma_start(w2_raw[:, SETS, :], sw2).then_inc(w_landed[2], 16)
            sp.dma_start(wqkv[:], wqkv_t).then_inc(attn_landed, 16)
            sp.dma_start(wout[:], wout_t).then_inc(attn_landed, 16)
            sp.dma_start(bout_rows[:], b_out.partition_broadcast(P)).then_inc(attn_landed, 16)
            sp.dma_start(ng[:], norm_g).then_inc(attn_landed, 16)
            sp.dma_start(nb[:], norm_b).then_inc(attn_landed, 16)

            for f in range(2):
                sp.wait_ge(c_rows_done, f + 1)
                sp.dma_start(c_dram[f].rearrange("e (t q) -> (e t) q", q=P), c_rows[:]).then_inc(c_stored, 16)
                sp.wait_ge(c_stored, 16 * (f + 1))

                def spread(e, p, b):
                    sp.dma_start(cb[p][:, SEQ * b:SEQ * b + SEQ],
                                 c_dram[f][bass.ds(e, 1), SEQ * b:SEQ * b + SEQ].broadcast_to([P, SEQ])
                                 ).then_inc(cb_landed[p][b], 16)

                for p in range(2):
                    for b in range(NB):
                        spread(p, p, b)
                sp.dma_start(cT[:], c_dram[f]).then_inc(cT_landed, 16)
                with sp.Fori(1, NE // 2) as i:
                    for p in range(2):
                        for b in range(NB):
                            sp.wait_ge(weighted, RF * f + 2 * NB * i + NB * (p - 2) + b + 1)
                            spread(2 * i + p, p, b)
            for b in range(NB):
                sp.wait_ge(resid, 2 * NB + b + 1)
                sp.dma_start(out_tok[:, TB * b:TB * b + TB, :], x[:, TB * b:TB * b + TB, :]).then_inc(stored, 16)
            sp.wait_ge(stored, 16 * NB)

        @block.gpsimd
        def _(pool):
            nc.gpsimd.memset(minus_half[:], -0.5)
            nc.gpsimd.memset(zeros[:], 0.0)
            for p in range(2):
                nc.gpsimd.memset(xn[p][:, :, D:D + 2], 1.0)
            for j in range(NE):
                nc.gpsimd.memset(tie_order[:, :, j], float(NE - j))
            nc.gpsimd.memset(head_mask[:], 1.0)
            nc.gpsimd.memset(ident[:], 0.0).then_inc(const_step, 1)
            pool.wait_ge(const_step, 1)
            nc.gpsimd.affine_select(out=ident[:], in_=ident[:], compare_op=ALU.not_equal, fill=1.0, base=0,
                                    pattern=[[-1, P]], channel_multiplier=1).then_inc(consts, 1)
            nc.gpsimd.affine_select(out=head_mask[:], in_=head_mask[:], compare_op=ALU.is_ge, fill=0.0, base=0,
                                    pattern=[[-HD, HEADS], [0, HD]], channel_multiplier=1).then_inc(const_step, 1)
            pool.wait_ge(const_step, 2)
            nc.gpsimd.affine_select(out=head_mask[:], in_=head_mask[:], compare_op=ALU.is_ge, fill=0.0,
                                    base=HD - 1, pattern=[[HD, HEADS], [0, HD]],
                                    channel_multiplier=-1).then_inc(consts, 1)

            def inverse_root(ln, k):
                pool.wait_ge(var_done, ln + 1)
                nc.gpsimd.tensor_tensor(rstd[:, k, :], var_eps[:, k, :], minus_half[:], ALU.pow).then_inc(rstd_done, 1)

            def split_w13(g, slot, p):
                pool.wait_ge(w13h_done, g + 1)
                nc.gpsimd.tensor_copy(bias13[p][:], bias_raw[:, bass.ds(slot, 1), :].rearrange("p a k -> p (a k)"))
                nc.gpsimd.tensor_tensor(w13l[p][:], w13_raw[:, bass.ds(slot, 1), :, :].rearrange("p a k o -> p (a k) o"),
                                        w13h[p][:].bitcast(F32), ALU.subtract).then_inc(w13l_done, 1)

            def split_w2(g, slot, p):
                pool.wait_ge(w2h_done, g + 1)
                nc.gpsimd.tensor_tensor(w2l[p][:], w2_raw[:, bass.ds(slot, 1), :].rearrange("p a o -> p (a o)"),
                                        w2h[p][:].bitcast(F32), ALU.subtract).then_inc(w2l_done, 1)

            def low_half(N, b):
                pool.wait_ge(hh_done, N + 1)
                nc.gpsimd.tensor_tensor(hl[b][:], u_t[b % 2][:], hh[b][:].bitcast(F32),
                                        ALU.subtract).then_inc(hl_odd, 1)

            for f in range(2):
                if f == 0:
                    for b in range(NB):
                        inverse_root(b, b % 2)
                        if b == 0:
                            split_w13(0, 0, 0)
                            split_w2(0, 0, 0)
                else:
                    for b in range(NB):
                        inverse_root(2 * NB + b, b % 2)
                g = SETS * f
                for b in range(NB):
                    if b % 2:
                        low_half(NB * g + b, b)
                    if b == 1:
                        split_w13(g + 1, 1, (g + 1) % 2)
                    if b == 3:
                        split_w2(g + 1, 1, (g + 1) % 2)
                with pool.Fori(0, NE // 2) as i:
                    for q in range(2):
                        gi = SETS * f + 1 + q + 2 * i
                        par = (SETS * f + 1 + q) % 2
                        for b in range(NB):
                            if b % 2:
                                low_half(UF * f + NB + NB * q + b + 2 * NB * i, b)
                            if b == 1:
                                split_w13(gi + 1, 2 * i + q + 2, 1 - par)
                            if b == 3:
                                split_w2(gi + 1, 2 * i + q + 2, 1 - par)
                if f == 0:
                    pool.wait_ge(attn_landed, 80)
                    with pool.Fori(0, NB // 2) as j:
                        for p in range(2):
                            inverse_root(NB + p + 2 * j, p)
                        for p in range(2):
                            pool.wait_ge(xn_done, NB + p + 1 + 2 * j)
                            xs = x[:, bass.ds(2 * TB * j + TB * p, TB), :]
                            nc.gpsimd.tensor_tensor(xs, xs, bout_rows[:].unsqueeze(1).broadcast_to([P, TB, D]),
                                                    ALU.add).then_inc(bout_added, 1)

        @block.scalar
        def _(act):
            def split_w13(g, slot, p, first=False):
                if not first:
                    act.wait_ge(lin_half, NB * g - NB)
                nc.scalar.copy(w13h[p][:], w13_raw[:, bass.ds(slot, 1), :, :].rearrange("p a k o -> p (a k) o")
                               ).then_inc(w13h_done, 1)

            def split_w2(g, slot, p, first=False):
                if not first:
                    act.wait_ge(down_done, NB * g - NB)
                nc.scalar.copy(w2h[p][:], w2_raw[:, bass.ds(slot, 1), :].rearrange("p a o -> p (a o)")
                               ).then_inc(w2h_done, 1)

            def silu(N, par, b):
                act.wait_ge(gate_half, N + 1)
                nc.scalar.activation(s_t[b % 2][:], work[2 * (b % 2)][:], ACT.Silu,
                                     bias=bias13[par][:, 0:1]).then_inc(silu_done, 1)

            def high_half(N, b):
                act.wait_ge(u_done, N + 1)
                nc.scalar.copy(hh[b][:], u_t[b % 2][:]).then_inc(hh_done, 1)

            for f in range(2):
                if f == 0:
                    act.wait_ge(small_landed, 64)
                    nc.scalar.copy(gate_h[:], gate_raw[:]).then_inc(gate_w_done, 1)
                    act.wait_ge(w_landed[0], 48)
                    split_w13(0, 0, 0, first=True)
                    split_w2(0, 0, 0, first=True)
                for b in range(NB):
                    act.wait_ge(xT_done, NB * f + b + 1)
                    if f == 1 and b == 0:
                        act.wait_ge(gate_half, UF)
                    nc.scalar.copy(xh[:, SEQ * b:SEQ * b + SEQ], work[b][:]).then_inc(xh_done, 1)
                act.wait_ge(gate_centred, f + 1)
                nc.scalar.activation(g_e[:], g_d[:], ACT.Exp).then_inc(gate_exp, 1)

                g = SETS * f
                for b in range(NB):
                    N = NB * g + b
                    if N >= 2:
                        act.wait_ge(u_done, N - 1)
                    silu(N, g % 2, b)
                    if b == 1:
                        act.wait_ge(w_landed[1], 48)
                        split_w13(g + 1, 1, (g + 1) % 2, first=g + 1 < 2)
                    if b == 3:
                        split_w2(g + 1, 1, (g + 1) % 2, first=g + 1 < 2)
                    if b >= 1:
                        if N - 1 >= NB:
                            act.wait_ge(down_done, N - NB)
                        high_half(N - 1, b - 1)
                act.wait_ge(c_tr_done, f + 1)
                nc.scalar.copy(c_rows[:], c_tr).then_inc(c_rows_done, 1)
                if f == 0:
                    act.wait_ge(w_landed[2], 96)
                with act.Fori(0, NE // 2) as i:
                    for q in range(2):
                        gi = SETS * f + 1 + q + 2 * i
                        par = (SETS * f + 1 + q) % 2
                        for b in range(NB):
                            N = UF * f + NB + NB * q + b + 2 * NB * i
                            act.wait_ge(u_done, N - 1)
                            silu(N, par, b)
                            if b == 1:
                                split_w13(gi + 1, 2 * i + q + 2, 1 - par)
                            if b == 3:
                                split_w2(gi + 1, 2 * i + q + 2, 1 - par)
                            act.wait_ge(down_done, N - NB)
                            high_half(N - 1, (b - 1) % NB)
                N = UF * f + UF
                act.wait_ge(down_done, N - NB)
                high_half(N - 1, NB - 1)
                for b in range(NB):
                    act.wait_ge(y_done, NB * f + b + 1)
                    nc.scalar.activation(yT[b][:], yps[b][:], ACT.Identity, bias=sb2s[:]).then_inc(yT_done, 1)

                if f == 0:
                    with act.Fori(0, NB // 2) as j:
                        for p in range(2):
                            act.wait_ge(a_xT_ps, 2 * j + p + 1)
                            nc.scalar.copy(a_xT[p][:], bank[p][0][:]).then_inc(a_xT_sb, 1)
                        for p in range(2):
                            act.wait_ge(a_Q_ps, 2 * j + p + 1)
                            nc.scalar.copy(a_Q[p][:], bank[p][3][:]).then_inc(a_Q_sb, 1)
                        for p in range(2):
                            act.wait_ge(a_n2_sb, 2 * j + p + 1)
                            nc.scalar.activation(a_nr[p][:], a_n2[p][:], ACT.Sqrt).then_inc(a_root, 1)
                        for p in range(2):
                            act.wait_ge(a_At_ps, 2 * j + p + 1)
                            nc.scalar.activation(a_aT[p][:], bank[p][1][:], ACT.Identity,
                                                 bias=a_bv[p][:]).then_inc(a_aT_sb, 1)

        @block.vector
        def _(dve):
            gate_steps = [0]
            dve.wait_ge(consts, 2)

            def ln_stats(ln, k, tile0, in_loop=False):
                for t in range(TB):
                    last = nc.vector.bn_stats(stats[:, k, t, :], x[:, bass.ds(tile0 + t, 1), :].rearrange("p a d -> p (a d)"))
                last.then_inc(stats_done, 1)
                dve.wait_ge(stats_done, ln + 1)
                if in_loop:
                    nc.vector.memset(wait_carrier[:], 0.0)
                for t in range(TB):
                    last = nc.vector.bn_aggr(moments[:, k, t, :], stats[:, k, t, :])
                last.then_inc(moments_done, 1)
                dve.wait_ge(moments_done, ln + 1)
                nc.vector.tensor_scalar(var_eps[:, k, :], moments[:, k, :, 1], LN_EPS, None,
                                        ALU.add).then_inc(var_done, 1)

            def ln_apply(ln, k, tile0):
                dve.wait_ge(rstd_done, ln + 1)
                for t in range(TB):
                    last = nc.vector.tensor_scalar(xn[k][:, t, 0:D],
                                                   x[:, bass.ds(tile0 + t, 1), :].rearrange("p a d -> p (a d)"),
                                                   moments[:, k, t, 0:1], rstd[:, k, t:t + 1],
                                                   ALU.subtract, ALU.mult)
                last.then_inc(xn_done, 1)

            def wide(a):
                return a[:].unsqueeze(2).broadcast_to([P, NT, NE])

            def gate(f):
                def link(ins):
                    gate_steps[0] += 1
                    ins.then_inc(gate_step, 1)
                    dve.wait_ge(gate_step, gate_steps[0])

                m, z, r, m1, k1, m2 = small
                lg = logits.rearrange("p (t e) -> p t e", e=NE)
                dve.wait_ge(logits_done, NB * (f + 1))
                link(nc.vector.tensor_reduce(m[:], lg, AX_X, ALU.max))
                nc.vector.tensor_tensor(g_d[:], lg, wide(m), ALU.subtract).then_inc(gate_centred, 1)
                dve.wait_ge(gate_exp, f + 1)
                link(nc.vector.tensor_reduce(z[:], g_e[:], AX_X, ALU.add))
                link(nc.vector.reciprocal(r[:], z[:]))
                link(nc.vector.tensor_tensor(g_p[:], g_e[:], wide(r), ALU.mult))
                link(nc.vector.tensor_reduce(m1[:], g_p[:], AX_X, ALU.max))
                link(nc.vector.tensor_tensor(g_v[:], g_p[:], wide(m1), ALU.is_equal))
                link(nc.vector.tensor_tensor(g_w[:], g_v[:], tie_order[:], ALU.mult))
                link(nc.vector.tensor_reduce(k1[:], g_w[:], AX_X, ALU.max))
                link(nc.vector.tensor_tensor(g_s1[:], g_w[:], wide(k1), ALU.is_equal))
                link(nc.vector.scalar_tensor_tensor(out=g_p2[:], in0=g_s1[:], scalar=-2.0, in1=g_p[:],
                                                    op0=ALU.mult, op1=ALU.add))
                link(nc.vector.tensor_reduce(m2[:], g_p2[:], AX_X, ALU.max))
                link(nc.vector.tensor_tensor(g_v[:], g_p2[:], wide(m2), ALU.is_equal))
                link(nc.vector.tensor_tensor(g_w[:], g_v[:], tie_order[:], ALU.mult))
                link(nc.vector.tensor_reduce(k1[:], g_w[:], AX_X, ALU.max))
                link(nc.vector.tensor_tensor(g_s2[:], g_w[:], wide(k1), ALU.is_equal))
                link(nc.vector.tensor_tensor(g_sel[:], g_s1[:], g_s2[:], ALU.add))
                nc.vector.tensor_tensor(g_c[:].rearrange("p e t -> p t e"), g_sel[:], g_p[:],
                                        ALU.mult).then_inc(combine_done, 1)

            def low_x(f, b):
                dve.wait_ge(xh_done, NB * f + b + 1)
                nc.vector.tensor_tensor(xl[:, SEQ * b:SEQ * b + SEQ], work[b][:],
                                        xh[:, SEQ * b:SEQ * b + SEQ].bitcast(F32), ALU.subtract).then_inc(xl_done, 1)

            def weigh(N, R, p, b, landed):
                dve.wait_ge(silu_done, N + 1)
                dve.wait_ge(cb_landed[p][b], landed)
                nc.vector.tensor_tensor(s_t[b % 2][:], s_t[b % 2][:], cb[p][:, SEQ * b:SEQ * b + SEQ],
                                        ALU.mult).then_inc(weighted, 1)

            def product(N, par, b, R=None):
                dve.wait_ge(lin_half, N + 1)
                if R is None:
                    dve.wait_ge(silu_done, N + 1)
                else:
                    dve.wait_ge(weighted, R + 1)
                nc.vector.scalar_tensor_tensor(out=u_t[b % 2][:], in0=work[2 * (b % 2) + 1][:],
                                               scalar=bias13[par][:, 1:2], in1=s_t[b % 2][:],
                                               op0=ALU.add, op1=ALU.mult).then_inc(u_done, 1)

            def low_half(N, b):
                dve.wait_ge(hh_done, N + 1)
                nc.vector.tensor_tensor(hl[b][:], u_t[b % 2][:], hh[b][:].bitcast(F32),
                                        ALU.subtract).then_inc(hl_even, 1)

            for f in range(2):
                ln0 = 2 * NB * f
                for b in range(NB + 1):
                    if b < NB:
                        if f == 0:
                            dve.wait_ge(x_in_sem[b], 16)
                        else:
                            dve.wait_ge(resid, NB + b + 1)
                        ln_stats(ln0 + b, b % 2, TB * b)
                    if b == 0 and f == 0:
                        dve.wait_ge(gate_w_done, 1)
                        nc.vector.tensor_tensor(gate_l[:], gate_raw[:], gate_h[:].bitcast(F32),
                                                ALU.subtract).then_inc(gate_w_done, 1)
                    if b >= 1:
                        if b >= 3:
                            dve.wait_ge(xT_done, NB * f + b - 2)
                        ln_apply(ln0 + b - 1, (b - 1) % 2, TB * (b - 1))
                    if b >= 2:
                        low_x(f, b - 2)
                low_x(f, NB - 1)
                gate(f)

                g = SETS * f
                for b in range(NB):
                    N = NB * g + b
                    if b >= 1 and (b - 1) % 2 == 0:
                        low_half(N - 1, b - 1)
                    if N >= 2:
                        dve.wait_ge(hh_done, N - 1)
                        dve.wait_ge(hl_odd if b % 2 else hl_even, N // 2)
                    product(N, g % 2, b)
                with dve.Fori(0, NE // 2) as i:
                    for q in range(2):
                        for b in range(NB):
                            N = UF * f + NB + NB * q + b + 2 * NB * i
                            R = RF * f + NB * q + b + 2 * NB * i
                            weigh(N, R, q, b, 16 * (NE // 2) * f + 16 * i + 16)
                            if (b - 1) % 2 == 0:
                                low_half(N - 1, b - 1)
                            dve.wait_ge(hh_done, N - 1)
                            dve.wait_ge(hl_odd if b % 2 else hl_even, (UF * f + NB + NB * q + b) // 2 + NB * i)
                            product(N, (SETS * f + 1 + q) % 2, b, R)

                for b in range(NB):
                    dve.wait_ge(y_back, NB * f + b + 1)
                    xs = x[:, TB * b:TB * b + TB, :]
                    nc.vector.scalar_tensor_tensor(out=xs, in0=work[b][:].rearrange("p (t d) -> p t d", d=D),
                                                   scalar=0.5, in1=xs, op0=ALU.mult,
                                                   op1=ALU.add).then_inc(resid, 1)
                if f == 1:
                    break

                with dve.Fori(0, NB // 2) as j:
                    for p in range(2):
                        dve.wait_ge(resid, 2 * j + p + 1)
                        ln_stats(NB + p + 2 * j, p, 2 * TB * j + TB * p, True)
                    for p in range(2):
                        ln_apply(NB + p + 2 * j, p, 2 * TB * j + TB * p)
                    for p in range(2):
                        dve.wait_ge(a_S_ps, 2 * j + p + 1)
                        nc.vector.tensor_copy(a_S[p][:], bank[p][1][:, 0:D + 2]).then_inc(a_S_sb, 1)
                    for p in range(2):
                        dve.wait_ge(a_T_ps, 2 * j + p + 1)
                        nc.vector.tensor_copy(a_T[p][:], bank[p][2][:, 0:2 * D])
                        nc.vector.tensor_scalar(a_bv[p][:], bank[p][2][:, 2 * D:2 * D + 1], nb[:, 0:1], None,
                                                ALU.mult).then_inc(a_T_sb, 1)
                    for p in range(2):
                        dve.wait_ge(a_GN_ps, 2 * j + p + 1)
                        hm = head_mask[:].rearrange("p h d -> p (h d)")
                        nc.vector.tensor_tensor(a_G[p][:], bank[p][1][:, 0:D], hm, ALU.mult)
                        nc.vector.scalar_tensor_tensor(out=a_N[p][:], in0=bank[p][1][:, D:2 * D],
                                                       scalar=ng[:, 0:1], in1=hm, op0=ALU.mult,
                                                       op1=ALU.mult).then_inc(a_GN_sb, 1)
                    for p in range(2):
                        dve.wait_ge(a_U_ps, 2 * j + p + 1)
                        nc.vector.tensor_tensor(a_P[p][:], bank[p][2][:], a_Q[p][:], ALU.mult).then_inc(a_P_sb, 1)
                    for p in range(2):
                        dve.wait_ge(a_n_ps, 2 * j + p + 1)
                        nc.vector.tensor_scalar(a_n2[p][:], bank[p][0][:, 0:TB * HEADS].rearrange(
                            "p (t h) -> p t h", h=HEADS), NORM_EPS * NORM_EPS, None, ALU.max).then_inc(a_n2_sb, 1)
                    for p in range(2):
                        dve.wait_ge(a_root, 2 * j + p + 1)
                        nc.vector.reciprocal(a_inv[p][:], a_nr[p][:]).then_inc(a_inv_sb, 1)
                    for p in range(2):
                        dve.wait_ge(a_inv_sb, 2 * j + p + 1)
                        dve.wait_ge(a_R_ps, 2 * j + p + 1)
                        nc.vector.tensor_tensor(
                            a_A[p][:].rearrange("p t (h d) -> p (t h) d", d=HD),
                            bank[p][3][:].rearrange("p (a d) -> p a d", d=HD),
                            a_inv[p][:].rearrange("p t h -> p (t h)").unsqueeze(2).broadcast_to([P, TB * HEADS, HD]),
                            ALU.mult).then_inc(a_A_sb, 1)
                    for p in range(2):
                        dve.wait_ge(a_O_ps, 2 * j + p + 1)
                        dve.wait_ge(bout_added, 2 * j + p + 1)
                        xs = x[:, bass.ds(2 * TB * j + TB * p, TB), :]
                        nc.vector.tensor_tensor(xs, bank[p][2][:].rearrange("p (t d) -> p t d", d=D), xs,
                                                ALU.add).then_inc(resid, 1)

        @block.tensor
        def _(pe):
            def triple(dst, wh, wl, rh, rl, start, stop):
                nc.tensor.matmul(dst, wh, rl, start=start, stop=False, skip_group_check=True)
                nc.tensor.matmul(dst, wh, rh, start=False, stop=False, skip_group_check=True)
                return nc.tensor.matmul(dst, wl, rh, start=False, stop=stop, skip_group_check=True)

            def up(N, g, par, b):
                xhb, xlb = xh[:, SEQ * b:SEQ * b + SEQ], xl[:, SEQ * b:SEQ * b + SEQ]
                if b == 0:
                    pe.wait_ge(w13l_done, g + 1)
                triple(work[2 * (b % 2)][:], w13h[par][:, 0, :], w13l[par][:, 0, :], xhb, xlb,
                       True, True).then_inc(gate_half, 1)
                triple(work[2 * (b % 2) + 1][:], w13h[par][:, 1, :], w13l[par][:, 1, :], xhb, xlb,
                       True, True).then_inc(lin_half, 1)

            def clear(b):
                nc.tensor.matmul(yps[b][:], zeros[:, 0:P], zeros[:], start=True, stop=False, skip_group_check=True)

            def down(N, g, par, b, lows):
                if b == 0:
                    pe.wait_ge(w2l_done, g + 1)
                pe.wait_ge(hl_odd if b % 2 else hl_even, lows)
                triple(yps[b][:], w2h[par][:], w2l[par][:], hh[b][:], hl[b][:], False, False).then_inc(down_done, 1)

            pe.wait_ge(consts, 2)
            for f in range(2):
                for b in range(NB):
                    ln = 2 * NB * f + b
                    pe.wait_ge(xn_done, ln + 1)
                    for t in range(TB):
                        last = nc.tensor.transpose(work[b][:, P * t:P * t + P], xn[b % 2][:, t, 0:D], ident[:])
                    last.then_inc(xT_done, 1)
                    for bb in ([b - 1] if b >= 1 else []) + ([b] if b == NB - 1 else []):
                        if f == 0 and bb == 0:
                            pe.wait_ge(gate_w_done, 2)
                        pe.wait_ge(xl_done, NB * f + bb + 1)
                        for t in range(TB * bb, TB * bb + TB):
                            dst = logits[:, NE * t:NE * t + NE]
                            sl = slice(P * t, P * t + P)
                            nc.tensor.matmul(dst, xl[:, sl], gate_h[:], start=True, stop=False)
                            nc.tensor.matmul(dst, xh[:, sl], gate_l[:], start=False, stop=False)
                            last = nc.tensor.matmul(dst, xh[:, sl], gate_h[:], start=False, stop=True)
                        last.then_inc(logits_done, 1)

                g = SETS * f
                par = g % 2
                for b in range(NB):
                    N = NB * g + b
                    if b >= 2 or f == 1:
                        pe.wait_ge(u_done, N - 1)
                    up(N, g, par, b)
                    if b >= 2:
                        clear(b - 2)
                        down(N - 2, g, par, b - 2, (N - 2) // 2 + 1)
                pe.wait_ge(combine_done, f + 1)
                nc.tensor.transpose(c_tr, g_c[:].rearrange("p e t -> p (e t)"), ident[:]).then_inc(c_tr_done, 1)
                clear(2)
                pe.wait_ge(c_rows_done, f + 1)
                clear(3)
                with pe.Fori(0, NE // 2) as i:
                    for q in range(2):
                        gi = SETS * f + 1 + q + 2 * i
                        par = (SETS * f + 1 + q) % 2
                        for b in range(NB):
                            n0 = UF * f + NB + NB * q + b
                            N = n0 + 2 * NB * i
                            pe.wait_ge(u_done, N - 1)
                            up(N, gi, par, b)
                            if b >= 2:
                                down(N - 2, gi, par, b - 2, (n0 - 2) // 2 + 1 + NB * i)
                            else:
                                down(N - 2, gi - 1, 1 - par, b + 2, (n0 - 2) // 2 + 1 + NB * i)
                N = UF * f + UF
                g = SETS * f + SETS - 1
                par = g % 2
                pe.wait_ge(cT_landed, 16 * (f + 1))

                def bias_of_experts(b):
                    nc.tensor.matmul(yps[b][:], b2s[:], cT[:, SEQ * b:SEQ * b + SEQ], start=False, stop=True,
                                     skip_group_check=True).then_inc(y_done, 1)

                bias_of_experts(0)
                bias_of_experts(1)
                for b in (2, 3):
                    down(N - NB + b, g, par, b, (N - NB + b) // 2 + 1)
                    bias_of_experts(b)
                for b in range(NB):
                    pe.wait_ge(yT_done, NB * f + b + 1)
                    pe.wait_ge(u_done, N)
                    for t in range(TB):
                        last = nc.tensor.transpose(work[b][:, P * t:P * t + P], yT[b][:, P * t:P * t + P], ident[:])
                    last.then_inc(y_back, 1)
                if f == 1:
                    break

                pe.wait_ge(attn_landed, 80)
                with pe.Fori(0, NB // 2) as j:
                    for p in range(2):
                        k = 2 * j + p
                        pe.wait_ge(xn_done, NB + k + 1)
                        for t in range(TB):
                            last = nc.tensor.transpose(bank[p][0][:, P * t:P * t + P], xn[p][:, t, 0:D], ident[:])
                        last.then_inc(a_xT_ps, 1)
                        for t in range(TB):
                            last = nc.tensor.matmul(bank[p][1][:, 0:D + 2], xn[p][:, t, 0:D], xn[p][:, t, :],
                                                    start=t == 0, stop=t == TB - 1)
                        last.then_inc(a_S_ps, 1)
                    for p in range(2):
                        k = 2 * j + p
                        pe.wait_ge(a_xT_sb, k + 1)
                        nc.tensor.matmul(bank[p][3][:], wqkv[:, 0:D], a_xT[p][:], start=True,
                                         stop=True).then_inc(a_Q_ps, 1)
                    for p in range(2):
                        k = 2 * j + p
                        pe.wait_ge(a_S_sb, k + 1)
                        nc.tensor.matmul(bank[p][2][:, 0:2 * D], a_S[p][:, 0:D], wqkv[:, D:3 * D], start=True, stop=True)
                        nc.tensor.matmul(bank[p][2][:, 2 * D:2 * D + 2], wqkv[:, 2 * D:3 * D], a_S[p][:, D:D + 2],
                                         start=True, stop=True).then_inc(a_T_ps, 1)
                    for p in range(2):
                        k = 2 * j + p
                        pe.wait_ge(a_T_sb, k + 1)
                        nc.tensor.matmul(bank[p][1][:, 0:2 * D], wqkv[:, D:2 * D], a_T[p][:], start=True,
                                         stop=True).then_inc(a_GN_ps, 1)
                    for p in range(2):
                        k = 2 * j + p
                        pe.wait_ge(a_GN_sb, k + 1)
                        pe.wait_ge(a_Q_sb, k + 1)
                        nc.tensor.matmul(bank[p][2][:], a_G[p][:], a_Q[p][:], start=True, stop=True).then_inc(a_U_ps, 1)
                        for t in range(TB):
                            last = nc.tensor.matmul(bank[p][3][:, P * t:P * t + P], a_Q[p][:, P * t:P * t + P], a_N[p][:],
                                                    start=True, stop=True)
                        last.then_inc(a_R_ps, 1)
                    for p in range(2):
                        k = 2 * j + p
                        pe.wait_ge(a_P_sb, k + 1)
                        for t in range(TB):
                            last = nc.tensor.matmul(bank[p][0][:, HEADS * t:HEADS * t + HEADS],
                                                    a_P[p][:, P * t:P * t + P], head_mask[:, :, 0],
                                                    start=True, stop=True)
                        last.then_inc(a_n_ps, 1)
                    for p in range(2):
                        k = 2 * j + p
                        pe.wait_ge(a_A_sb, k + 1)
                        for t in range(TB):
                            last = nc.tensor.transpose(bank[p][1][:, P * t:P * t + P], a_A[p][:, t, :], ident[:])
                        last.then_inc(a_At_ps, 1)
                    for p in range(2):
                        k = 2 * j + p
                        pe.wait_ge(a_aT_sb, k + 1)
                        for t in range(TB):
                            last = nc.tensor.matmul(bank[p][2][:, P * t:P * t + P], a_aT[p][:, P * t:P * t + P], wout[:],
                                                    start=True, stop=True)
                        last.then_inc(a_O_ps, 1)


def kernel(**inputs):
    import numpy as _np
    import concourse.bacc as _bacc
    from concourse import mybir as _mybir
    from concourse.bass_utils import run_bass_kernel_spmd as _run

    a = {k: _np.asarray(v) for k, v in inputs.items()}
    x = a["L0_attn_x"]
    d = x.shape[2]
    heads = a["L0_attn_norm_g"].size
    laid = {
        "x": x,
        "wqkv_t": a["L0_attn_w_qkv"].T,
        "wout_t": a["L0_attn_w_out"].T,
        "b_out": a["L0_attn_b_out"],
        "norm_g": _np.repeat(a["L0_attn_norm_g"].reshape(heads), d // heads).reshape(d, 1),
        "norm_b": _np.repeat(a["L0_attn_norm_b"].reshape(heads), d // heads).reshape(d, 1),
        "gate_t": a["L0_ffn_gate_w"].T,
        "w1": a["L0_ffn_w1"],
        "bias_t": _np.stack([_np.vstack([a[f"L0_ffn_sb{k}"], a[f"L0_ffn_b{k}"], a[f"L0_ffn_sb{k}"]]).T
                             for k in (1, 3)], axis=2),
        "w2": a["L0_ffn_w2"],
        "b2": a["L0_ffn_b2"],
        "w3": a["L0_ffn_w3"],
        "sw1": a["L0_ffn_sw1"],
        "sw2": a["L0_ffn_sw2"],
        "sb2": a["L0_ffn_sb2"].reshape(d, 1),
        "sw3": a["L0_ffn_sw3"],
    }
    nc = _bacc.Bacc("TRN2", target_bir_lowering=False, num_devices=1)
    arrays, args = {}, []
    for name, v in laid.items():
        v = _np.ascontiguousarray(v)
        arrays[f"in_{name}"] = v
        args.append(nc.dram_tensor(f"in_{name}", v.shape, _mybir.dt.from_np(v.dtype), kind="ExternalInput").ap())
    args.append(nc.dram_tensor("out_0", x.shape, _mybir.dt.from_np(x.dtype), kind="ExternalOutput").ap())
    macaron_kernel(nc, *args, heads)
    r = _run(nc, [arrays], core_ids=[0])
    return r.results[0]["out_0"]
```

```python
from contextlib import ExitStack

import concourse.bass as bass
from concourse import mybir

F32 = mybir.dt.float32
F32R = mybir.dt.float32r
ALU = mybir.AluOpType
ACT = mybir.ActivationFunctionType
AX_X = mybir.AxisListType.X

P = 128
LN_EPS = 1e-5
NORM_EPS = 1e-12


def macaron_kernel(
    nc: bass.Bass,
    x_in: bass.AP,
    wqkv_t: bass.AP,
    wout_t: bass.AP,
    b_out: bass.AP,
    norm_g: bass.AP,
    norm_b: bass.AP,
    gate_t: bass.AP,
    w1: bass.AP,
    bias_t: bass.AP,
    w2: bass.AP,
    b2: bass.AP,
    w3: bass.AP,
    sw1: bass.AP,
    sw2: bass.AP,
    sb2: bass.AP,
    sw3: bass.AP,
    out: bass.AP,
    heads: int,
):
    NB, SEQ, D = x_in.shape
    NE = w1.shape[0]
    HEADS = heads
    HD = D // HEADS
    TOK = NB * SEQ
    TB = SEQ // P
    NT = NB * TB
    SETS = NE + 1
    assert D == P and w1.shape[2] == P and NB == 4 and SEQ == 512 and NE % 2 == 0 and NT * NE == P and SEQ == TB * P

    SECTIONS = 4
    PB = NB // 2
    PT = PB * TB
    U = SETS * PB
    PTOK = PB * SEQ

    c_dram = [nc.dram_tensor(f"combine_{k}", (NE, PTOK), F32, kind="Internal").ap() for k in range(SECTIONS)]

    with ExitStack() as ctx:
        def sb(name, shape, dt=F32):
            return ctx.enter_context(nc.sbuf_tensor(name, shape, dt))

        def psum(name, shape):
            return ctx.enter_context(nc.psum_tensor(name, shape, F32))

        def sem(name):
            return ctx.enter_context(nc.semaphore(name))

        x = sb("x", [P, NT, D])
        xh = sb("xh", [P, TOK], F32R)
        xl = sb("xl", [P, TOK], F32R)
        w13_raw = sb("w13_raw", [P, SETS + 1, 2, P])
        w2_raw = sb("w2_raw", [P, SETS + 1, P])
        w13h = [sb(f"w13h{p}", [P, 2, P], F32R) for p in range(2)]
        w13l = [sb(f"w13l{p}", [P, 2, P], F32R) for p in range(2)]
        w2h = [sb(f"w2h{p}", [P, P], F32R) for p in range(2)]
        w2l = [sb(f"w2l{p}", [P, P], F32R) for p in range(2)]
        bias_raw = sb("bias_raw", [P, SETS + 1, 2])
        bias13 = [sb(f"bias13{p}", [P, 2]) for p in range(2)]
        b2s = sb("b2s", [NE, P])
        sb2s = sb("sb2s", [P, 1])
        gate_raw = sb("gate_raw", [P, NE])
        gate_h = sb("gate_h", [P, NE], F32R)
        gate_l = sb("gate_l", [P, NE], F32R)
        wqkv = sb("wqkv", [P, 3 * D])
        wout = sb("wout", [P, D])
        bout_rows = sb("bout_rows", [P, D])
        ng = sb("ng", [P, 1])
        nb = sb("nb", [P, 1])
        ident = sb("ident", [P, P])
        head_mask = sb("head_mask", [P, HEADS, HD])
        tie_order = sb("tie_order", [P, PT, NE])
        minus_half = sb("minus_half", [P, TB])
        stats = sb("stats", [P, 2, TB, 6])
        moments = sb("moments", [P, 2, TB, 2])
        var_eps = sb("var_eps", [P, 2, TB])
        rstd = sb("rstd", [P, 2, TB])
        neg_mean = sb("neg_mean", [P, 2, TB])
        xn = [sb(f"xn{p}", [P, TB, D + 2]) for p in range(2)]
        small = [sb(f"small{k}", [P, PT]) for k in range(6)]
        g_d, g_e, g_p, g_w, g_v, g_s1, g_p2, g_s2, g_sel = (
            sb(name, [P, PT, NE]) for name in ("g_d", "g_e", "g_p", "g_w", "g_v", "g_s1", "g_p2", "g_s2", "g_sel"))
        g_c = sb("g_c", [P, NE, PT])
        c_rows = sb("c_rows", [NE * PT, P])
        cT = [sb(f"cT{k}", [NE, PTOK]) for k in range(2)]
        cb = [[sb(f"cb{p}{q}", [P, SEQ]) for q in range(PB)] for p in range(2)]
        s_t = [sb(f"s_t{k}", [P, SEQ]) for k in range(2)]
        u_t = [sb(f"u_t{k}", [P, SEQ]) for k in range(2)]
        hh = [sb(f"hh{k}", [P, SEQ], F32R) for k in range(4)]
        hl = [sb(f"hl{k}", [P, SEQ], F32R) for k in range(4)]
        yT = [sb(f"yT{k}", [P, SEQ]) for k in range(PB)]
        a_xT = [sb(f"a_xT{p}", [P, SEQ]) for p in range(2)]
        a_S = [sb(f"a_S{p}", [P, D + 2]) for p in range(2)]
        a_T = [sb(f"a_T{p}", [P, 2 * D]) for p in range(2)]
        a_bv = [sb(f"a_bv{p}", [P, 1]) for p in range(2)]
        a_G = [sb(f"a_G{p}", [P, D]) for p in range(2)]
        a_N = [sb(f"a_N{p}", [P, D]) for p in range(2)]
        a_Q = [sb(f"a_Q{p}", [P, SEQ]) for p in range(2)]
        a_P = [sb(f"a_P{p}", [P, SEQ]) for p in range(2)]
        a_n2 = [sb(f"a_n2{p}", [P, TB, HEADS]) for p in range(2)]
        a_nr = [sb(f"a_nr{p}", [P, TB, HEADS]) for p in range(2)]
        a_inv = [sb(f"a_inv{p}", [P, TB, HEADS]) for p in range(2)]
        a_A = [sb(f"a_A{p}", [P, TB, D]) for p in range(2)]
        a_aT = [sb(f"a_aT{p}", [P, SEQ]) for p in range(2)]

        work = [psum(f"work{k}", [P, 512]) for k in range(4)]
        yps = [psum(f"yps{k}", [P, 512]) for k in range(4)]

        x_landed = [sem(f"x_landed{b}") for b in range(NB)]
        w_landed = [sem(f"w_landed{k}") for k in range(3)]
        small_landed = sem("small_landed")
        attn_landed = sem("attn_landed")
        const_step = sem("const_step")
        consts = sem("consts")
        stats_done = sem("stats_done")
        moments_done = sem("moments_done")
        var_done = sem("var_done")
        rstd_done = sem("rstd_done")
        xn_done = sem("xn_done")
        xT_done = sem("xT_done")
        xh_done = sem("xh_done")
        xl_done = sem("xl_done")
        gate_w_done = sem("gate_w_done")
        logits_done = sem("logits_done")
        gate_step = sem("gate_step")
        gate_centred = sem("gate_centred")
        gate_exp = sem("gate_exp")
        combine_done = sem("combine_done")
        c_tr_done = sem("c_tr_done")
        c_rows_done = sem("c_rows_done")
        c_stored = sem("c_stored")
        cT_landed = [sem(f"cT_landed{k}") for k in range(2)]
        cb_landed = [[sem(f"cb_landed{p}{q}") for q in range(PB)] for p in range(2)]
        w13h_done = sem("w13h_done")
        w13l_done = sem("w13l_done")
        biases_done = sem("biases_done")
        w2h_done = sem("w2h_done")
        w2l_done = sem("w2l_done")
        gate_half = sem("gate_half")
        lin_half = sem("lin_half")
        silu_done = sem("silu_done")
        weighted = sem("weighted")
        u_done = sem("u_done")
        hh_done = sem("hh_done")
        hl_even = sem("hl_even")
        hl_odd = sem("hl_odd")
        down_done = sem("down_done")
        y_done = sem("y_done")
        yT_done = sem("yT_done")
        y_back = sem("y_back")
        resid = sem("resid")
        bout_added = sem("bout_added")
        a_S_ps, a_S_sb = sem("a_S_ps"), sem("a_S_sb")
        a_xT_ps, a_xT_sb = sem("a_xT_ps"), sem("a_xT_sb")
        a_T_ps, a_T_sb = sem("a_T_ps"), sem("a_T_sb")
        a_GN_ps, a_GN_sb = sem("a_GN_ps"), sem("a_GN_sb")
        a_Q_ps, a_Q_sb = sem("a_Q_ps"), sem("a_Q_sb")
        a_U_ps, a_P_sb = sem("a_U_ps"), sem("a_P_sb")
        a_n_ps, a_n2_sb = sem("a_n_ps"), sem("a_n2_sb")
        a_root, a_inv_sb = sem("a_root"), sem("a_inv_sb")
        a_R_ps, a_A_sb = sem("a_R_ps"), sem("a_A_sb")
        a_At_ps, a_aT_sb = sem("a_At_ps"), sem("a_aT_sb")
        a_O_ps = sem("a_O_ps")
        stored = sem("stored")

        BESIDE = {
            3: [("leave", 0)], 4: [("back", 0), ("norm1", 0)], 5: [("leave", 1)], 6: [("back", 1), ("norm1", 1)],
            9: [("xx", 0)], 10: [("turn", 0)], 11: [("xxw", 0), ("xx", 1)], 12: [("kk", 0), ("turn", 1)],
            13: [("q", 0), ("xxw", 1)], 14: [("kkq", 0), ("kk", 1)], 15: [("square", 0), ("q", 1)],
            16: [("qkv", 0), ("kkq", 1)], 17: [("square", 1), ("root", 0), ("root", 1)],
            18: [("scale", 0), ("qkv", 1)], 19: [("turn_out", 0), ("scale", 1)],
            20: [("project", 0), ("turn_out", 1)], 21: [("norm2", 0), ("project", 1)], 22: [("norm2", 1)],
            25: [("enter", 0)], 26: [("logits", 0), ("enter", 1)], 27: [("logits", 1), ("exp", 0)],
            28: [("gate", 0)], 29: [("gate", 1)], 30: [("gate", 2)], 31: [("gate", 3)], 32: [("weights", 0)],
        }
        BESIDE_LAST = {3: [("leave", 0)], 4: [("back", 0)], 5: [("leave", 1)], 6: [("back", 1)]}
        BESIDE_FIRST = {4: [("exp", 0)], 5: [("gate", 0)], 6: [("gate", 1)], 7: [("gate", 2)], 8: [("gate", 3)],
                        9: [("weights", 0)]}
        PEELED = 3 * PB
        LAG = 3

        def beside(sec, slot):
            return (BESIDE_FIRST, BESIDE, BESIDE, BESIDE_LAST)[sec].get(slot, [])

        def place_of(sec, place, i):
            return U * sec + place + 4 * i, SETS * sec + place // PB + 2 * i, place // PB + 2 * i

        def batch_of(sec, place):
            return PB * (sec % 2) + place % PB

        x_tok = x_in.rearrange("b s d -> (b s) d").rearrange("(t p) d -> p t d", p=P)
        out_tok = out.rearrange("b s d -> (b s) d").rearrange("(t p) d -> p t d", p=P)

        def run_section(engine, sec, unit):
            straight = U if sec in (1, 2) else PEELED
            for place in range(straight):
                unit(sec, place, 0)
            if straight < U:
                with engine.Fori(1, (U - PB) // 4) as i:
                    for place in range(PB, PEELED):
                        unit(sec, place, i)

        block = ctx.enter_context(nc.Block())

        @block.sync
        def _(sp):
            def load_x(b):
                sp.dma_start(x[:, TB * b:TB * b + TB, :], x_tok[:, TB * b:TB * b + TB, :]).then_inc(x_landed[b], 16)

            load_x(0)
            load_x(1)
            sp.dma_start(gate_raw[:], gate_t).then_inc(small_landed, 16)
            sp.dma_start(bias_raw[:], bias_t).then_inc(small_landed, 16)
            sp.dma_start(b2s[:], b2).then_inc(small_landed, 16)
            sp.dma_start(sb2s[:], sb2).then_inc(small_landed, 16)
            sp.dma_start(w13_raw[:, 0, 0, :], sw1).then_inc(w_landed[0], 16)
            sp.dma_start(w13_raw[:, 0, 1, :], sw3).then_inc(w_landed[0], 16)
            sp.dma_start(w2_raw[:, 0, :], sw2).then_inc(w_landed[0], 16)
            load_x(2)
            load_x(3)
            for k, (e0, e1) in enumerate([(0, 2), (2, NE)]):
                for w, dst in ((w1, w13_raw[:, 1 + e0:1 + e1, 0, :]), (w3, w13_raw[:, 1 + e0:1 + e1, 1, :]),
                               (w2, w2_raw[:, 1 + e0:1 + e1, :])):
                    sp.dma_start(dst, w[e0:e1].rearrange("e i o -> i e o")).then_inc(w_landed[1 + k], 16)
            sp.dma_start(w13_raw[:, SETS, 0, :], sw1).then_inc(w_landed[2], 16)
            sp.dma_start(w13_raw[:, SETS, 1, :], sw3).then_inc(w_landed[2], 16)
            sp.dma_start(w2_raw[:, SETS, :], sw2).then_inc(w_landed[2], 16)
            sp.dma_start(wqkv[:], wqkv_t).then_inc(attn_landed, 16)
            sp.dma_start(wout[:], wout_t).then_inc(attn_landed, 16)
            sp.dma_start(bout_rows[:], b_out.partition_broadcast(P)).then_inc(attn_landed, 16)
            sp.dma_start(ng[:], norm_g).then_inc(attn_landed, 16)
            sp.dma_start(nb[:], norm_b).then_inc(attn_landed, 16)

            for sec in range(SECTIONS):
                sp.wait_ge(c_rows_done, sec + 1)
                sp.dma_start(c_dram[sec].rearrange("e (t q) -> (e t) q", q=P), c_rows[:]).then_inc(c_stored, 16)
                sp.wait_ge(c_stored, 16 * (sec + 1))

                def spread(e, p, q):
                    routed = PB * NE * sec + PB * e + q
                    if not isinstance(routed, int) or routed >= 2 * PB:
                        sp.wait_ge(weighted, routed - 2 * PB + 1)
                    sp.dma_start(cb[p][q][:], c_dram[sec][bass.ds(e, 1), SEQ * q:SEQ * q + SEQ].broadcast_to([P, SEQ])
                                 ).then_inc(cb_landed[p][q], 16)

                for e in range(2):
                    for q in range(PB):
                        spread(e, e, q)
                if sec >= 2:
                    sp.wait_ge(y_done, PB * (sec - 1))
                sp.dma_start(cT[sec % 2][:], c_dram[sec]).then_inc(cT_landed[sec % 2], 16)
                with sp.Fori(1, NE // 2) as i:
                    for p in range(2):
                        for q in range(PB):
                            spread(2 * i + p, p, q)
            for b in range(NB):
                sp.wait_ge(resid, 2 * NB + b + 1)
                sp.dma_start(out_tok[:, TB * b:TB * b + TB, :], x[:, TB * b:TB * b + TB, :]).then_inc(stored, 16)
            sp.wait_ge(stored, 16 * NB)

        @block.gpsimd
        def _(pool):
            nc.gpsimd.memset(minus_half[:], -0.5)
            for p in range(2):
                nc.gpsimd.memset(xn[p][:, :, D:D + 2], 1.0)
            nc.gpsimd.memset(ident[:], 0.0).then_inc(const_step, 1)
            pool.wait_ge(const_step, 1)
            nc.gpsimd.affine_select(out=ident[:], in_=ident[:], compare_op=ALU.not_equal, fill=1.0, base=0,
                                    pattern=[[-1, P]], channel_multiplier=1).then_inc(consts, 1)

            def inverse_root(ln):
                k = ln % 2
                pool.wait_ge(var_done, ln + 1)
                nc.gpsimd.tensor_tensor(rstd[:, k, :], var_eps[:, k, :], minus_half[:], ALU.pow).then_inc(rstd_done, 1)

            def normalise(ln, b):
                k = ln % 2
                pool.wait_ge(rstd_done, ln + 1)
                for t in range(TB):
                    last = nc.gpsimd.tensor_scalar(xn[k][:, t, 0:D], x[:, TB * b + t, :], neg_mean[:, k, t:t + 1],
                                                   rstd[:, k, t:t + 1], ALU.add, ALU.mult)
                last.then_inc(xn_done, 1)

            def split_w13(g, slot, p):
                pool.wait_ge(w13h_done, g + 1)
                nc.gpsimd.tensor_tensor(w13l[p][:], w13_raw[:, bass.ds(slot, 1), :, :].rearrange("p a k o -> p (a k) o"),
                                        w13h[p][:].bitcast(F32), ALU.subtract).then_inc(w13l_done, 1)

            def take_biases(slot, p):
                nc.gpsimd.tensor_copy(bias13[p][:], bias_raw[:, bass.ds(slot, 1), :].rearrange("p a k -> p (a k)")
                                      ).then_inc(biases_done, 1)

            def split_w2(g, slot, p):
                pool.wait_ge(w2h_done, g + 1)
                nc.gpsimd.tensor_tensor(w2l[p][:], w2_raw[:, bass.ds(slot, 1), :].rearrange("p a o -> p (a o)"),
                                        w2h[p][:].bitcast(F32), ALU.subtract).then_inc(w2l_done, 1)

            def low_half(n, n0):
                pool.wait_ge(hh_done, n + 1)
                nc.gpsimd.tensor_tensor(hl[n0 % 4][:], u_t[n0 % 2][:], hh[n0 % 4][:].bitcast(F32),
                                        ALU.subtract).then_inc(hl_odd, 1)

            def side(sec, slot):
                for job, p in beside(sec, slot):
                    b = PB * ((sec - 1) % 2) + p
                    kk = PB * (sec - 1) + p
                    if job == "norm1":
                        inverse_root(2 * kk - p + NB)
                        normalise(2 * kk - p + NB, b)
                        pool.wait_ge(xn_done, 2 * kk - p + NB + 1)
                        xs = x[:, TB * b:TB * b + TB, :]
                        nc.gpsimd.tensor_tensor(xs, xs, bout_rows[:].unsqueeze(1).broadcast_to([P, TB, D]),
                                                ALU.add).then_inc(bout_added, 1)
                    if job == "norm2":
                        inverse_root(2 * kk - p + NB + PB)
                        normalise(2 * kk - p + NB + PB, b)

            def unit(sec, place, i):
                n, g, slot = place_of(sec, place, i)
                g0 = SETS * sec + place // PB
                if place % PB == 0:
                    split_w13(g + 1, slot + 1, (g0 + 1) % 2)
                    if not (sec == 0 and place == 0):
                        low_half(n - 1, U * sec + place - 1)
                    take_biases(slot + 1, (g0 + 1) % 2)
                elif g0 >= 1:
                    split_w2(g, slot, g0 % 2)
                if isinstance(i, int):
                    side(sec, 2 * place)
                    side(sec, 2 * place + 1)

            inverse_root(0)
            inverse_root(1)
            split_w13(0, 0, 0)
            pool.wait_ge(small_landed, 64)
            take_biases(0, 0)
            split_w2(0, 0, 0)
            for j in range(NE):
                nc.gpsimd.memset(tie_order[:, :, j], float(NE - j))
            nc.gpsimd.memset(head_mask[:], 1.0).then_inc(const_step, 1)
            pool.wait_ge(const_step, 2)
            nc.gpsimd.affine_select(out=head_mask[:], in_=head_mask[:], compare_op=ALU.is_ge, fill=0.0, base=0,
                                    pattern=[[-HD, HEADS], [0, HD]], channel_multiplier=1).then_inc(const_step, 1)
            pool.wait_ge(const_step, 3)
            nc.gpsimd.affine_select(out=head_mask[:], in_=head_mask[:], compare_op=ALU.is_ge, fill=0.0,
                                    base=HD - 1, pattern=[[HD, HEADS], [0, HD]],
                                    channel_multiplier=-1).then_inc(consts, 1)
            inverse_root(2)
            inverse_root(3)
            for sec in range(SECTIONS):
                if sec == 1:
                    pool.wait_ge(attn_landed, 80)
                run_section(pool, sec, unit)
            low_half(SECTIONS * U - 1, SECTIONS * U - 1)

        @block.scalar
        def _(act):
            def split_w13(g, slot, p, n):
                if not isinstance(n, int) or n >= 2:
                    act.wait_ge(lin_half, n)
                nc.scalar.copy(w13h[p][:], w13_raw[:, bass.ds(slot, 1), :, :].rearrange("p a k o -> p (a k) o")
                               ).then_inc(w13h_done, 1)

            def split_w2(g, slot, p, n):
                if not isinstance(n, int) or n > LAG:
                    act.wait_ge(down_done, n - LAG)
                nc.scalar.copy(w2h[p][:], w2_raw[:, bass.ds(slot, 1), :].rearrange("p a o -> p (a o)")
                               ).then_inc(w2h_done, 1)

            def high_half(n, n0):
                if not isinstance(n, int) or n >= 4:
                    act.wait_ge(down_done, n - 3)
                act.wait_ge(u_done, n + 1)
                nc.scalar.copy(hh[n0 % 4][:], u_t[n0 % 2][:]).then_inc(hh_done, 1)

            def enter(count, b):
                act.wait_ge(xT_done, count + 1)
                nc.scalar.copy(xh[:, SEQ * b:SEQ * b + SEQ], yps[b][:]).then_inc(xh_done, 1)

            def exp(gate_no):
                act.wait_ge(gate_centred, PB * gate_no + PB)
                nc.scalar.activation(g_e[:], g_d[:], ACT.Exp).then_inc(gate_exp, 1)

            def rows(gate_no, b):
                act.wait_ge(c_tr_done, gate_no + 1)
                if gate_no >= 1:
                    act.wait_ge(c_stored, 16 * gate_no)
                nc.scalar.copy(c_rows[:], yps[b][0:NE * PT, 0:P]).then_inc(c_rows_done, 1)

            def side(sec, slot):
                for job, p in beside(sec, slot):
                    b = PB * ((sec - 1) % 2) + p
                    kk = PB * (sec - 1) + p
                    if job == "leave":
                        act.wait_ge(y_done, kk + 1)
                        nc.scalar.activation(yT[p][:], yps[b][:], ACT.Identity, bias=sb2s[:]).then_inc(yT_done, 1)
                    if job == "xx":
                        act.wait_ge(a_S_ps, kk + 1)
                        nc.scalar.copy(a_S[p][:], yps[b][:, 0:D + 2]).then_inc(a_S_sb, 1)
                    if job == "turn":
                        act.wait_ge(a_xT_ps, kk + 1)
                        nc.scalar.copy(a_xT[p][:], yps[b][:]).then_inc(a_xT_sb, 1)
                    if job == "xxw":
                        act.wait_ge(a_T_ps, kk + 1)
                        nc.scalar.copy(a_T[p][:], yps[b][:, 0:2 * D])
                        nc.scalar.activation(a_bv[p][:], yps[b][:, 2 * D:2 * D + 1], ACT.Copy,
                                             scale=nb[:, 0:1]).then_inc(a_T_sb, 1)
                    if job == "q":
                        act.wait_ge(a_Q_ps, kk + 1)
                        nc.scalar.copy(a_Q[p][:], yps[b][:]).then_inc(a_Q_sb, 1)
                    if job == "root":
                        act.wait_ge(a_n2_sb, kk + 1)
                        nc.scalar.activation(a_nr[p][:], a_n2[p][:], ACT.Sqrt).then_inc(a_root, 1)
                    if job == "turn_out":
                        act.wait_ge(a_At_ps, kk + 1)
                        nc.scalar.activation(a_aT[p][:], yps[b][:], ACT.Identity, bias=a_bv[p][:]).then_inc(a_aT_sb, 1)
                    if job == "enter":
                        enter(NB + kk, b)
                    if job == "exp":
                        exp(sec + 1)
                    if job == "weights":
                        rows(sec + 1, PB * ((sec + 1) % 2))

            def unit(sec, place, i):
                n, g, slot = place_of(sec, place, i)
                n0, g0 = U * sec + place, SETS * sec + place // PB
                if place % PB == 0:
                    act.wait_ge(biases_done, g + 1)
                act.wait_ge(gate_half, n + 1)
                if n0 >= 2:
                    act.wait_ge(u_done, n - 1)
                nc.scalar.activation(s_t[n0 % 2][:], work[2 * (n0 % 2)][:], ACT.Silu,
                                     bias=bias13[g0 % 2][:, 0:1]).then_inc(silu_done, 1)
                if place % PB == 0:
                    if sec == 0 and place == 0:
                        act.wait_ge(w_landed[1], 48)
                    if sec == 0 and place == 2 * PB:
                        act.wait_ge(w_landed[2], 96)
                    split_w13(g + 1, slot + 1, (g0 + 1) % 2, n)
                elif g0 >= 1:
                    split_w2(g, slot, g0 % 2, n)
                if isinstance(i, int):
                    side(sec, 2 * place)
                if n0 >= 1:
                    high_half(n - 1, n0 - 1)
                if isinstance(i, int):
                    side(sec, 2 * place + 1)

            act.wait_ge(small_landed, 64)
            nc.scalar.copy(gate_h[:], gate_raw[:]).then_inc(gate_w_done, 1)
            act.wait_ge(w_landed[0], 48)
            split_w13(0, 0, 0, 0)
            split_w2(0, 0, 0, 0)
            enter(0, 0)
            enter(1, 1)
            exp(0)
            rows(0, 0)
            enter(2, 2)
            enter(3, 3)
            for sec in range(SECTIONS):
                run_section(act, sec, unit)
            high_half(SECTIONS * U - 1, SECTIONS * U - 1)
            for p in range(PB):
                act.wait_ge(y_done, 3 * PB + p + 1)
                nc.scalar.activation(yT[p][:], yps[PB + p][:], ACT.Identity, bias=sb2s[:]).then_inc(yT_done, 1)

        @block.vector
        def _(dve):
            gate_steps = [0]

            def ln_stats(ln, b):
                k = ln % 2
                if ln >= NB:
                    dve.wait_ge(xn_done, ln - 1)
                for t in range(TB):
                    last = nc.vector.bn_stats(stats[:, k, t, :], x[:, TB * b + t, :])
                last.then_inc(stats_done, 1)
                dve.wait_ge(stats_done, ln + 1)
                for t in range(TB):
                    last = nc.vector.bn_aggr(moments[:, k, t, :], stats[:, k, t, :])
                last.then_inc(moments_done, 1)
                dve.wait_ge(moments_done, ln + 1)
                nc.vector.tensor_scalar(neg_mean[:, k, :], moments[:, k, :, 0], -1.0, None, ALU.mult)
                nc.vector.tensor_scalar(var_eps[:, k, :], moments[:, k, :, 1], LN_EPS, None,
                                        ALU.add).then_inc(var_done, 1)

            def ln_apply(ln, b):
                k = ln % 2
                dve.wait_ge(rstd_done, ln + 1)
                for t in range(TB):
                    last = nc.vector.tensor_scalar(xn[k][:, t, 0:D], x[:, TB * b + t, :], moments[:, k, t, 0:1],
                                                   rstd[:, k, t:t + 1], ALU.subtract, ALU.mult)
                last.then_inc(xn_done, 1)

            def link(ins):
                gate_steps[0] += 1
                ins.then_inc(gate_step, 1)
                dve.wait_ge(gate_step, gate_steps[0])

            m, z, r, m1, k1, m2 = small

            def wide(a):
                return a[:].unsqueeze(2).broadcast_to([P, PT, NE])

            def centre(count, b, p):
                lg = yps[b][:, 0:TB * NE].rearrange("p (t e) -> p t e", e=NE)
                ts = slice(TB * p, TB * p + TB)
                dve.wait_ge(logits_done, count + 1)
                link(nc.vector.tensor_reduce(m[:, ts], lg, AX_X, ALU.max))
                nc.vector.tensor_tensor(g_d[:, ts, :], lg, m[:, ts].unsqueeze(2).broadcast_to([P, TB, NE]),
                                        ALU.subtract).then_inc(gate_centred, 1)

            def gate(part, gate_no):
                if part == 0:
                    dve.wait_ge(gate_exp, gate_no + 1)
                    link(nc.vector.tensor_reduce(z[:], g_e[:], AX_X, ALU.add))
                    link(nc.vector.reciprocal(r[:], z[:]))
                    link(nc.vector.tensor_tensor(g_p[:], g_e[:], wide(r), ALU.mult))
                    link(nc.vector.tensor_reduce(m1[:], g_p[:], AX_X, ALU.max))
                if part == 1:
                    link(nc.vector.tensor_tensor(g_v[:], g_p[:], wide(m1), ALU.is_equal))
                    link(nc.vector.tensor_tensor(g_w[:], g_v[:], tie_order[:], ALU.mult))
                    link(nc.vector.tensor_reduce(k1[:], g_w[:], AX_X, ALU.max))
                    link(nc.vector.tensor_tensor(g_s1[:], g_w[:], wide(k1), ALU.is_equal))
                if part == 2:
                    link(nc.vector.scalar_tensor_tensor(out=g_p2[:], in0=g_s1[:], scalar=-2.0, in1=g_p[:],
                                                        op0=ALU.mult, op1=ALU.add))
                    link(nc.vector.tensor_reduce(m2[:], g_p2[:], AX_X, ALU.max))
                    link(nc.vector.tensor_tensor(g_v[:], g_p2[:], wide(m2), ALU.is_equal))
                    link(nc.vector.tensor_tensor(g_w[:], g_v[:], tie_order[:], ALU.mult))
                if part == 3:
                    link(nc.vector.tensor_reduce(k1[:], g_w[:], AX_X, ALU.max))
                    link(nc.vector.tensor_tensor(g_s2[:], g_w[:], wide(k1), ALU.is_equal))
                    link(nc.vector.tensor_tensor(g_sel[:], g_s1[:], g_s2[:], ALU.add))
                    nc.vector.tensor_tensor(g_c[:].rearrange("p e t -> p t e"), g_sel[:], g_p[:],
                                            ALU.mult).then_inc(combine_done, 1)

            def low_x(count, b):
                dve.wait_ge(xh_done, count + 1)
                nc.vector.tensor_tensor(xl[:, SEQ * b:SEQ * b + SEQ], yps[b][:],
                                        xh[:, SEQ * b:SEQ * b + SEQ].bitcast(F32), ALU.subtract).then_inc(xl_done, 1)

            def add_back(count, b):
                dve.wait_ge(y_back, count + 1)
                xs = x[:, TB * b:TB * b + TB, :]
                nc.vector.scalar_tensor_tensor(out=xs, in0=yps[b][:].rearrange("p (t d) -> p t d", d=D),
                                               scalar=0.5, in1=xs, op0=ALU.mult, op1=ALU.add).then_inc(resid, 1)

            def side(sec, slot):
                for job, p in beside(sec, slot):
                    b = PB * ((sec - 1) % 2) + p
                    kk = PB * (sec - 1) + p
                    if job == "back":
                        add_back(kk, b)
                    if job == "norm1":
                        dve.wait_ge(resid, 2 * kk - p + 1)
                        ln_stats(2 * kk - p + NB, b)
                    if job == "kk":
                        dve.wait_ge(a_GN_ps, kk + 1)
                        hm = head_mask[:].rearrange("p h d -> p (h d)")
                        nc.vector.tensor_tensor(a_G[p][:], yps[b][:, 0:D], hm, ALU.mult)
                        nc.vector.scalar_tensor_tensor(out=a_N[p][:], in0=yps[b][:, D:2 * D], scalar=ng[:, 0:1],
                                                       in1=hm, op0=ALU.mult, op1=ALU.mult).then_inc(a_GN_sb, 1)
                    if job == "kkq":
                        dve.wait_ge(a_U_ps, kk + 1)
                        nc.vector.tensor_tensor(a_P[p][:], yps[b][:], a_Q[p][:], ALU.mult).then_inc(a_P_sb, 1)
                    if job == "square":
                        dve.wait_ge(a_n_ps, kk + 1)
                        nc.vector.tensor_scalar(a_n2[p][:], yps[b][:, 0:TB * HEADS].rearrange(
                            "p (t h) -> p t h", h=HEADS), NORM_EPS * NORM_EPS, None, ALU.max).then_inc(a_n2_sb, 1)
                    if job == "root":
                        dve.wait_ge(a_root, kk + 1)
                        nc.vector.reciprocal(a_inv[p][:], a_nr[p][:]).then_inc(a_inv_sb, 1)
                    if job == "scale":
                        dve.wait_ge(a_inv_sb, kk + 1)
                        dve.wait_ge(a_R_ps, kk + 1)
                        nc.vector.tensor_tensor(
                            a_A[p][:].rearrange("p t (h d) -> p (t h) d", d=HD),
                            yps[b][:].rearrange("p (a d) -> p a d", d=HD),
                            a_inv[p][:].rearrange("p t h -> p (t h)").unsqueeze(2).broadcast_to([P, TB * HEADS, HD]),
                            ALU.mult).then_inc(a_A_sb, 1)
                    if job == "project":
                        dve.wait_ge(a_O_ps, kk + 1)
                        dve.wait_ge(bout_added, kk + 1)
                        xs = x[:, TB * b:TB * b + TB, :]
                        nc.vector.tensor_tensor(xs, yps[b][:].rearrange("p (t d) -> p t d", d=D), xs,
                                                ALU.add).then_inc(resid, 1)
                    if job == "norm2":
                        dve.wait_ge(resid, 2 * kk - p + PB + 1)
                        ln_stats(2 * kk - p + NB + PB, b)
                    if job == "enter":
                        low_x(NB + kk, b)
                    if job == "logits":
                        centre(NB + kk, b, p)
                    if job == "gate":
                        gate(p, sec + 1)

            def low_half(n, n0):
                dve.wait_ge(hh_done, n + 1)
                nc.vector.tensor_tensor(hl[n0 % 4][:], u_t[n0 % 2][:], hh[n0 % 4][:].bitcast(F32),
                                        ALU.subtract).then_inc(hl_even, 1)

            def unit(sec, place, i):
                n, g, slot = place_of(sec, place, i)
                n0, g0 = U * sec + place, SETS * sec + place // PB
                e0, q = place // PB - 1, place % PB
                if e0 >= 0:
                    routed = PB * NE * sec + PB * e0 + q
                    dve.wait_ge(silu_done, n + 1)
                    dve.wait_ge(cb_landed[e0 % 2][q], 16 * (NE // 2 * sec + e0 // 2 + 1) + 16 * i)
                    nc.vector.tensor_tensor(s_t[n0 % 2][:], s_t[n0 % 2][:], cb[e0 % 2][q][:],
                                            ALU.mult).then_inc(weighted, 1)
                if isinstance(i, int):
                    side(sec, 2 * place)
                if n0 >= 1 and (n0 - 1) % 2 == 0:
                    low_half(n - 1, n0 - 1)
                dve.wait_ge(lin_half, n + 1)
                if e0 >= 0:
                    dve.wait_ge(weighted, routed + 1 + 4 * i)
                else:
                    dve.wait_ge(silu_done, n + 1)
                if n0 >= 2:
                    dve.wait_ge(hh_done, n - 1)
                    dve.wait_ge(hl_odd if n0 % 2 else hl_even, n0 // 2 + 2 * i)
                nc.vector.scalar_tensor_tensor(out=u_t[n0 % 2][:], in0=work[2 * (n0 % 2) + 1][:],
                                               scalar=bias13[g0 % 2][:, 1:2], in1=s_t[n0 % 2][:],
                                               op0=ALU.add, op1=ALU.mult).then_inc(u_done, 1)
                if isinstance(i, int):
                    side(sec, 2 * place + 1)

            dve.wait_ge(x_landed[0], 16)
            ln_stats(0, 0)
            dve.wait_ge(x_landed[1], 16)
            ln_stats(1, 1)
            ln_apply(0, 0)
            dve.wait_ge(gate_w_done, 1)
            nc.vector.tensor_tensor(gate_l[:], gate_raw[:], gate_h[:].bitcast(F32),
                                    ALU.subtract).then_inc(gate_w_done, 1)
            ln_apply(1, 1)
            low_x(0, 0)
            low_x(1, 1)
            centre(0, 0, 0)
            centre(1, 1, 1)
            dve.wait_ge(consts, 2)
            for part in range(4):
                gate(part, 0)
            for b in (2, 3):
                dve.wait_ge(x_landed[b], 16)
                ln_stats(b, b)
            for b in (2, 3):
                dve.wait_ge(xT_done, b - 1)
                ln_apply(b, b)
            low_x(2, 2)
            low_x(3, 3)
            centre(2, 2, 0)
            centre(3, 3, 1)
            for sec in range(SECTIONS):
                run_section(dve, sec, unit)
            for p in range(PB):
                add_back(3 * PB + p, PB + p)

        @block.tensor
        def _(pe):
            def triple(dst, wh, wl, rh, rl, start, stop):
                nc.tensor.matmul(dst, wh, rl, start=start, stop=False, skip_group_check=True)
                nc.tensor.matmul(dst, wh, rh, start=False, stop=False, skip_group_check=True)
                return nc.tensor.matmul(dst, wl, rh, start=False, stop=stop, skip_group_check=True)

            def turn(dst, tile):
                for t in range(TB):
                    last = nc.tensor.transpose(dst[:, P * t:P * t + P], tile(t), ident[:])
                return last

            def logits(count, b):
                pe.wait_ge(xl_done, count + 1)
                for t in range(TB):
                    dst = yps[b][:, NE * t:NE * t + NE]
                    sl = slice(SEQ * b + P * t, SEQ * b + P * t + P)
                    nc.tensor.matmul(dst, xl[:, sl], gate_h[:], start=True, stop=False)
                    nc.tensor.matmul(dst, xh[:, sl], gate_l[:], start=False, stop=False)
                    last = nc.tensor.matmul(dst, xh[:, sl], gate_h[:], start=False, stop=True)
                last.then_inc(logits_done, 1)

            def turn_weights(gate_no, b):
                pe.wait_ge(combine_done, gate_no + 1)
                nc.tensor.transpose(yps[b][0:NE * PT, 0:P], g_c[:].rearrange("p e t -> p (e t)"),
                                    ident[:]).then_inc(c_tr_done, 1)

            def down(m, sec, place, i):
                if place < 0 and isinstance(i, int):
                    sec, place = sec - 1, place + U
                m0, g0 = U * sec + place, SETS * sec + place // PB
                b = batch_of(sec, place)
                if place % PB == 0:
                    pe.wait_ge(w2l_done, g0 + 2 * i + 1)
                pe.wait_ge(hl_odd if m0 % 2 else hl_even, m0 // 2 + 1 + 2 * i)
                first = isinstance(i, int) and place < PB
                triple(yps[b][:], w2h[g0 % 2][:], w2l[g0 % 2][:], hh[m0 % 4][:], hl[m0 % 4][:],
                       first, False).then_inc(down_done, 1)
                if isinstance(i, int) and place >= U - PB:
                    q = place % PB
                    pe.wait_ge(cT_landed[sec % 2], 16 * (sec // 2 + 1))
                    nc.tensor.matmul(yps[b][:], b2s[:], cT[sec % 2][:, SEQ * q:SEQ * q + SEQ], start=False, stop=True,
                                     skip_group_check=True).then_inc(y_done, 1)

            def side(sec, slot):
                for job, p in beside(sec, slot):
                    b = PB * ((sec - 1) % 2) + p
                    kk = PB * (sec - 1) + p
                    y = yps[PB * ((sec - 1) % 2) + p % PB]
                    if job == "back":
                        pe.wait_ge(yT_done, kk + 1)
                        turn(y, lambda t: yT[p][:, P * t:P * t + P]).then_inc(y_back, 1)
                    if job == "xx":
                        pe.wait_ge(xn_done, 2 * kk - p + NB + 1)
                        for t in range(TB):
                            last = nc.tensor.matmul(y[:, 0:D + 2], xn[p][:, t, 0:D], xn[p][:, t, :],
                                                    start=t == 0, stop=t == TB - 1)
                        last.then_inc(a_S_ps, 1)
                    if job == "turn":
                        pe.wait_ge(a_S_sb, kk + 1)
                        turn(y, lambda t: xn[p][:, t, 0:D]).then_inc(a_xT_ps, 1)
                    if job == "xxw":
                        pe.wait_ge(a_xT_sb, kk + 1)
                        nc.tensor.matmul(y[:, 0:2 * D], a_S[p][:, 0:D], wqkv[:, D:3 * D], start=True, stop=True)
                        nc.tensor.matmul(y[:, 2 * D:2 * D + 2], wqkv[:, 2 * D:3 * D], a_S[p][:, D:D + 2],
                                         start=True, stop=True).then_inc(a_T_ps, 1)
                    if job == "kk":
                        pe.wait_ge(a_T_sb, kk + 1)
                        nc.tensor.matmul(y[:, 0:2 * D], wqkv[:, D:2 * D], a_T[p][:], start=True,
                                         stop=True).then_inc(a_GN_ps, 1)
                    if job == "q":
                        pe.wait_ge(a_GN_sb, kk + 1)
                        nc.tensor.matmul(y[:], wqkv[:, 0:D], a_xT[p][:], start=True, stop=True).then_inc(a_Q_ps, 1)
                    if job == "kkq":
                        pe.wait_ge(a_Q_sb, kk + 1)
                        nc.tensor.matmul(y[:], a_G[p][:], a_Q[p][:], start=True, stop=True).then_inc(a_U_ps, 1)
                    if job == "square":
                        pe.wait_ge(a_P_sb, kk + 1)
                        for t in range(TB):
                            last = nc.tensor.matmul(y[:, HEADS * t:HEADS * t + HEADS], a_P[p][:, P * t:P * t + P],
                                                    head_mask[:, :, 0], start=True, stop=True)
                        last.then_inc(a_n_ps, 1)
                    if job == "qkv":
                        pe.wait_ge(a_n2_sb, kk + 1)
                        for t in range(TB):
                            last = nc.tensor.matmul(y[:, P * t:P * t + P], a_Q[p][:, P * t:P * t + P], a_N[p][:],
                                                    start=True, stop=True)
                        last.then_inc(a_R_ps, 1)
                    if job == "turn_out":
                        pe.wait_ge(a_A_sb, kk + 1)
                        turn(y, lambda t: a_A[p][:, t, :]).then_inc(a_At_ps, 1)
                    if job == "project":
                        pe.wait_ge(a_aT_sb, kk + 1)
                        for t in range(TB):
                            last = nc.tensor.matmul(y[:, P * t:P * t + P], a_aT[p][:, P * t:P * t + P], wout[:],
                                                    start=True, stop=True)
                        last.then_inc(a_O_ps, 1)
                    if job == "enter":
                        pe.wait_ge(xn_done, 2 * kk - p + NB + PB + 1)
                        turn(y, lambda t: xn[p][:, t, 0:D]).then_inc(xT_done, 1)
                    if job == "logits":
                        logits(NB + kk, b)
                    if job == "weights":
                        turn_weights(sec + 1, PB * ((sec + 1) % 2))

            def unit(sec, place, i):
                n, g, slot = place_of(sec, place, i)
                n0, g0 = U * sec + place, SETS * sec + place // PB
                b = batch_of(sec, place)
                if place % PB == 0:
                    pe.wait_ge(w13l_done, g + 1)
                if place < PB:
                    pe.wait_ge(xl_done, PB * sec + place + 1)
                if n0 >= 2:
                    pe.wait_ge(u_done, n - 1)
                xhb, xlb = xh[:, SEQ * b:SEQ * b + SEQ], xl[:, SEQ * b:SEQ * b + SEQ]
                wh, wl = w13h[g0 % 2], w13l[g0 % 2]
                triple(work[2 * (n0 % 2)][:], wh[:, 0, :], wl[:, 0, :], xhb, xlb, True, True).then_inc(gate_half, 1)
                triple(work[2 * (n0 % 2) + 1][:], wh[:, 1, :], wl[:, 1, :], xhb, xlb, True, True).then_inc(lin_half, 1)
                if isinstance(i, int):
                    side(sec, 2 * place)
                if not (isinstance(i, int) and n0 < LAG):
                    down(n - LAG, sec, place - LAG, i)
                if isinstance(i, int):
                    side(sec, 2 * place + 1)

            pe.wait_ge(consts, 1)
            for b in range(2):
                pe.wait_ge(xn_done, b + 1)
                turn(yps[b], lambda t: xn[b][:, t, 0:D]).then_inc(xT_done, 1)
            pe.wait_ge(gate_w_done, 2)
            logits(0, 0)
            logits(1, 1)
            turn_weights(0, 0)
            for b in range(2, 4):
                pe.wait_ge(xn_done, b + 1)
                turn(yps[b], lambda t: xn[b % 2][:, t, 0:D]).then_inc(xT_done, 1)
            logits(2, 2)
            logits(3, 3)
            for sec in range(SECTIONS):
                if sec == 1:
                    pe.wait_ge(attn_landed, 80)
                run_section(pe, sec, unit)
            for k in range(LAG):
                down(0, SECTIONS, k - LAG, 0)
            for p in range(PB):
                pe.wait_ge(yT_done, 3 * PB + p + 1)
                turn(yps[PB + p], lambda t: yT[p][:, P * t:P * t + P]).then_inc(y_back, 1)


def kernel(**inputs):
    import numpy as _np
    import concourse.bacc as _bacc
    from concourse import mybir as _mybir
    from concourse.bass_utils import run_bass_kernel_spmd as _run

    a = {k: _np.asarray(v) for k, v in inputs.items()}
    x = a["L0_attn_x"]
    d = x.shape[2]
    heads = a["L0_attn_norm_g"].size
    laid = {
        "x": x,
        "wqkv_t": a["L0_attn_w_qkv"].T,
        "wout_t": a["L0_attn_w_out"].T,
        "b_out": a["L0_attn_b_out"],
        "norm_g": _np.repeat(a["L0_attn_norm_g"].reshape(heads), d // heads).reshape(d, 1),
        "norm_b": _np.repeat(a["L0_attn_norm_b"].reshape(heads), d // heads).reshape(d, 1),
        "gate_t": a["L0_ffn_gate_w"].T,
        "w1": a["L0_ffn_w1"],
        "bias_t": _np.stack([_np.vstack([a[f"L0_ffn_sb{k}"], a[f"L0_ffn_b{k}"], a[f"L0_ffn_sb{k}"]]).T
                             for k in (1, 3)], axis=2),
        "w2": a["L0_ffn_w2"],
        "b2": a["L0_ffn_b2"],
        "w3": a["L0_ffn_w3"],
        "sw1": a["L0_ffn_sw1"],
        "sw2": a["L0_ffn_sw2"],
        "sb2": a["L0_ffn_sb2"].reshape(d, 1),
        "sw3": a["L0_ffn_sw3"],
    }
    nc = _bacc.Bacc("TRN2", target_bir_lowering=False, num_devices=1)
    arrays, args = {}, []
    for name, v in laid.items():
        v = _np.ascontiguousarray(v)
        arrays[f"in_{name}"] = v
        args.append(nc.dram_tensor(f"in_{name}", v.shape, _mybir.dt.from_np(v.dtype), kind="ExternalInput").ap())
    args.append(nc.dram_tensor("out_0", x.shape, _mybir.dt.from_np(x.dtype), kind="ExternalOutput").ap())
    macaron_kernel(nc, *args, heads)
    r = _run(nc, [arrays], core_ids=[0])
    return r.results[0]["out_0"]
```
